# Optimizing a Trainium2 kernel written in Bass

```python
import numpy as np
import jax
import jax.numpy as jnp

def _softmax(x, axis=-1):
    return jax.nn.softmax(x, axis=axis)

def _gelu(x):
    return jax.nn.gelu(x, approximate=True)

def _silu(x):
    return jax.nn.silu(x)

def _sigmoid(x):
    return jax.nn.sigmoid(x)

def _layernorm(x, axis=-1, eps=1e-05):
    m = jnp.mean(x, axis=axis, keepdims=True)
    v = jnp.var(x, axis=axis, keepdims=True)
    return (x - m) / jnp.sqrt(v + eps)

def _scatter_add(tgt, idx, src, axis=0):
    return tgt.at[idx].add(src)

def _segment_sum(src, seg, n):
    return jax.ops.segment_sum(src, seg, n)
kernel_name = 'mk_dlrm_tower_d1_rec_r8_3bea3f'

def setup_inputs(seed: int=0):
    np.random.seed(seed)
    _w = jnp.asarray

    def _rec_inputs():
        import jax
        import jax.numpy as jnp
        _tk = jax.random.key(seed)
        ids = jnp.stack([jax.random.randint(jax.random.fold_in(_tk, 200 + f), (2048,), 0, v, jnp.int32) for f, v in enumerate([12500, 125000, 1250, 12500, 12500, 12500, 1250, 12500, 1250, 12500, 1000, 1250, 12500, 1250, 1000, 1250, 12500, 1000, 1000, 1000, 1000, 1250, 1250, 1250, 1000, 1000])], axis=1)
        tbl_0 = 0.05 * jax.random.normal(jax.random.fold_in(_tk, 500 + 0), (12500, 128), jnp.float32)
        tbl_1 = 0.05 * jax.random.normal(jax.random.fold_in(_tk, 500 + 1), (125000, 128), jnp.float32)
        tbl_2 = 0.05 * jax.random.normal(jax.random.fold_in(_tk, 500 + 2), (1250, 128), jnp.float32)
        tbl_3 = 0.05 * jax.random.normal(jax.random.fold_in(_tk, 500 + 3), (12500, 128), jnp.float32)
        tbl_4 = 0.05 * jax.random.normal(jax.random.fold_in(_tk, 500 + 4), (12500, 128), jnp.float32)
        tbl_5 = 0.05 * jax.random.normal(jax.random.fold_in(_tk, 500 + 5), (12500, 128), jnp.float32)
        tbl_6 = 0.05 * jax.random.normal(jax.random.fold_in(_tk, 500 + 6), (1250, 128), jnp.float32)
        tbl_7 = 0.05 * jax.random.normal(jax.random.fold_in(_tk, 500 + 7), (12500, 128), jnp.float32)
        tbl_8 = 0.05 * jax.random.normal(jax.random.fold_in(_tk, 500 + 8), (1250, 128), jnp.float32)
        tbl_9 = 0.05 * jax.random.normal(jax.random.fold_in(_tk, 500 + 9), (12500, 128), jnp.float32)
        tbl_10 = 0.05 * jax.random.normal(jax.random.fold_in(_tk, 500 + 10), (1000, 128), jnp.float32)
        tbl_11 = 0.05 * jax.random.normal(jax.random.fold_in(_tk, 500 + 11), (1250, 128), jnp.float32)
        tbl_12 = 0.05 * jax.random.normal(jax.random.fold_in(_tk, 500 + 12), (12500, 128), jnp.float32)
        tbl_13 = 0.05 * jax.random.normal(jax.random.fold_in(_tk, 500 + 13), (1250, 128), jnp.float32)
        tbl_14 = 0.05 * jax.random.normal(jax.random.fold_in(_tk, 500 + 14), (1000, 128), jnp.float32)
        tbl_15 = 0.05 * jax.random.normal(jax.random.fold_in(_tk, 500 + 15), (1250, 128), jnp.float32)
        tbl_16 = 0.05 * jax.random.normal(jax.random.fold_in(_tk, 500 + 16), (12500, 128), jnp.float32)
        tbl_17 = 0.05 * jax.random.normal(jax.random.fold_in(_tk, 500 + 17), (1000, 128), jnp.float32)
        tbl_18 = 0.05 * jax.random.normal(jax.random.fold_in(_tk, 500 + 18), (1000, 128), jnp.float32)
        tbl_19 = 0.05 * jax.random.normal(jax.random.fold_in(_tk, 500 + 19), (1000, 128), jnp.float32)
        tbl_20 = 0.05 * jax.random.normal(jax.random.fold_in(_tk, 500 + 20), (1000, 128), jnp.float32)
        tbl_21 = 0.05 * jax.random.normal(jax.random.fold_in(_tk, 500 + 21), (1250, 128), jnp.float32)
        tbl_22 = 0.05 * jax.random.normal(jax.random.fold_in(_tk, 500 + 22), (1250, 128), jnp.float32)
        tbl_23 = 0.05 * jax.random.normal(jax.random.fold_in(_tk, 500 + 23), (1250, 128), jnp.float32)
        tbl_24 = 0.05 * jax.random.normal(jax.random.fold_in(_tk, 500 + 24), (1000, 128), jnp.float32)
        tbl_25 = 0.05 * jax.random.normal(jax.random.fold_in(_tk, 500 + 25), (1000, 128), jnp.float32)
        _rk = jax.random.fold_in(_tk, 7)
        r_dense_features = -0.000520686 + 1.00062 * jax.random.normal(jax.random.fold_in(_rk, 101), (2048, 128), jnp.float32)
        W_top1 = 0.0405887 * jax.random.normal(jax.random.fold_in(_tk, 801), (607, 512), jnp.float32)
        W_top2 = 0.0441942 * jax.random.normal(jax.random.fold_in(_tk, 802), (512, 256), jnp.float32)
        W_top3 = 0.0625 * jax.random.normal(jax.random.fold_in(_tk, 803), (256, 1), jnp.float32)
        b_top1 = jnp.zeros((512,), jnp.float32)
        b_top2 = jnp.zeros((256,), jnp.float32)
        return (r_dense_features, ids, tbl_0, tbl_1, tbl_2, tbl_3, tbl_4, tbl_5, tbl_6, tbl_7, tbl_8, tbl_9, tbl_10, tbl_11, tbl_12, tbl_13, tbl_14, tbl_15, tbl_16, tbl_17, tbl_18, tbl_19, tbl_20, tbl_21, tbl_22, tbl_23, tbl_24, tbl_25, W_top1, b_top1, W_top2, b_top2, W_top3)
    r_dense_features, ids, tbl_0, tbl_1, tbl_2, tbl_3, tbl_4, tbl_5, tbl_6, tbl_7, tbl_8, tbl_9, tbl_10, tbl_11, tbl_12, tbl_13, tbl_14, tbl_15, tbl_16, tbl_17, tbl_18, tbl_19, tbl_20, tbl_21, tbl_22, tbl_23, tbl_24, tbl_25, W_top1, b_top1, W_top2, b_top2, W_top3 = _rec_inputs()

    def _L0_rec_setup():
        import jax, jax.numpy as jnp
        import numpy as np
        F = 26
        B, D = (2048, 128)
        _IU0, _IU1 = np.triu_indices(F + 1, k=1)
        _IU0 = jnp.asarray(_IU0)
        _IU1 = jnp.asarray(_IU1)
        key = jax.random.key(seed)
        k1, k2 = jax.random.split(key)
        dense_features = jax.random.normal(k1, (B, D), dtype=jnp.float32)
        sparse_features = jax.random.normal(k2, (B, F, D), dtype=jnp.float32)
        return {'dense_features': dense_features, 'sparse_features': sparse_features}
    _L0_rec_all = _L0_rec_setup()
    _L0_rec_in = {k: v for k, v in _L0_rec_all.items() if k in ()}
    del _L0_rec_all
    return {'r_dense_features': r_dense_features, 'ids': ids, 'tbl_0': tbl_0, 'tbl_1': tbl_1, 'tbl_2': tbl_2, 'tbl_3': tbl_3, 'tbl_4': tbl_4, 'tbl_5': tbl_5, 'tbl_6': tbl_6, 'tbl_7': tbl_7, 'tbl_8': tbl_8, 'tbl_9': tbl_9, 'tbl_10': tbl_10, 'tbl_11': tbl_11, 'tbl_12': tbl_12, 'tbl_13': tbl_13, 'tbl_14': tbl_14, 'tbl_15': tbl_15, 'tbl_16': tbl_16, 'tbl_17': tbl_17, 'tbl_18': tbl_18, 'tbl_19': tbl_19, 'tbl_20': tbl_20, 'tbl_21': tbl_21, 'tbl_22': tbl_22, 'tbl_23': tbl_23, 'tbl_24': tbl_24, 'tbl_25': tbl_25, 'W_top1': W_top1, 'b_top1': b_top1, 'W_top2': W_top2, 'b_top2': b_top2, 'W_top3': W_top3}

def reference(r_dense_features, ids, tbl_0, tbl_1, tbl_2, tbl_3, tbl_4, tbl_5, tbl_6, tbl_7, tbl_8, tbl_9, tbl_10, tbl_11, tbl_12, tbl_13, tbl_14, tbl_15, tbl_16, tbl_17, tbl_18, tbl_19, tbl_20, tbl_21, tbl_22, tbl_23, tbl_24, tbl_25, W_top1, b_top1, W_top2, b_top2, W_top3):
    import jax
    import jax.numpy as jnp

    def _L0_rec_ref(dense_features, sparse_features):
        import jax, jax.numpy as jnp
        import numpy as np
        F = 26
        B, D = (2048, 128)
        _IU0, _IU1 = np.triu_indices(F + 1, k=1)
        _IU0 = jnp.asarray(_IU0)
        _IU1 = jnp.asarray(_IU1)
        combined = jnp.concatenate([dense_features[:, None, :], sparse_features], axis=1)
        interactions = jnp.einsum('bfd,bgd->bfg', combined, combined)
        interactions_flat = interactions[:, _IU0, _IU1]
        return jnp.concatenate([dense_features, interactions_flat], axis=1)
    e = jnp.stack([tbl_0[ids[:, 0]], tbl_1[ids[:, 1]], tbl_2[ids[:, 2]], tbl_3[ids[:, 3]], tbl_4[ids[:, 4]], tbl_5[ids[:, 5]], tbl_6[ids[:, 6]], tbl_7[ids[:, 7]], tbl_8[ids[:, 8]], tbl_9[ids[:, 9]], tbl_10[ids[:, 10]], tbl_11[ids[:, 11]], tbl_12[ids[:, 12]], tbl_13[ids[:, 13]], tbl_14[ids[:, 14]], tbl_15[ids[:, 15]], tbl_16[ids[:, 16]], tbl_17[ids[:, 17]], tbl_18[ids[:, 18]], tbl_19[ids[:, 19]], tbl_20[ids[:, 20]], tbl_21[ids[:, 21]], tbl_22[ids[:, 22]], tbl_23[ids[:, 23]], tbl_24[ids[:, 24]], tbl_25[ids[:, 25]]], axis=1)
    z = _L0_rec_ref(r_dense_features, e)
    z = z.reshape(z.shape[0], -1)
    h = jnp.concatenate([z, r_dense_features], axis=1)
    h = jnp.maximum(h @ W_top1 + b_top1, 0.0)
    h = jnp.maximum(h @ W_top2 + b_top2, 0.0)
    y = h @ W_top3
    return y

_drawn_inputs = setup_inputs


def setup_inputs(seed=0):
    import zlib

    import numpy as np

    out = dict(_drawn_inputs(seed))
    spreads = {'b_top1': (0.0, 0.1), 'b_top2': (0.0, 0.1)}
    factors = {}
    for name, (base, spread) in spreads.items():
        noise = np.random.default_rng([zlib.crc32(name.encode()), seed]).standard_normal(out[name].shape)
        drawn = base * np.exp(spread * noise) if base else spread * noise
        out[name] = jnp.asarray(drawn.astype(out[name].dtype))
    for name, factor in factors.items():
        out[name] = (out[name] * factor).astype(out[name].dtype)
    return out
```

```python
import numpy as np
import concourse.bass as bass
import concourse.mybir as mybir
from contextlib import ExitStack

FP32 = mybir.dt.float32
FP32R = mybir.dt.float32r
INT32 = mybir.dt.int32
UINT32 = mybir.dt.uint32
ALU = mybir.AluOpType
ACT = mybir.ActivationFunctionType

BATCH, D = 2048, 128
TABLE_ROWS = [12500, 125000, 1250, 12500, 12500, 12500, 1250, 12500, 1250, 12500, 1000, 1250, 12500,
              1250, 1000, 1250, 12500, 1000, 1000, 1000, 1000, 1250, 1250, 1250, 1000, 1000]
N_TABLES = len(TABLE_ROWS)
HID1, HID2 = 512, 256

ONEHOT_ROWS = 1000
ONEHOT = [f for f in range(N_TABLES) if TABLE_ROWS[f] == ONEHOT_ROWS][:7]
GATHERED = [f for f in range(N_TABLES) if f not in ONEHOT]
NO, NG = len(ONEHOT), len(GATHERED)
F = 1 + N_TABLES
ORDER = [0] + [1 + f for f in GATHERED] + [1 + f for f in ONEHOT]

TILE = 128
TILES = BATCH // TILE
SC = 4
SUPERS = TILES // SC
SCB = SC * TILE
S4 = 4
GRP = TILE // S4
KROWS = 125
KT = ONEHOT_ROWS // KROWS
HALF = F // 2
JEXT = F + HALF
PI = 9
NP3 = F // PI
PAIRS = PI * HALF

TRF = 4
NTR = -(-NG // TRF)
GPB = 4
NGR = GRP // GPB
RING = 4


def dlrm_tower(nc, dense_t, idx_rows, ids_onehot, tables, w_dense, w_pairs, b1, w2, b2, w3, out):
    ctx = ExitStack()
    with ctx:
        def sb(name, shape, dt=FP32):
            return ctx.enter_context(nc.sbuf_tensor(name, shape, dt))

        def ps(name, shape):
            return ctx.enter_context(nc.psum_tensor(name, shape, FP32))

        def sem(name):
            return ctx.enter_context(nc.semaphore(name))

        rows = sb("rows", [128, SC, NG, D])
        idx_all = sb("idx_all", [128, TILES * NG], INT32)
        idx = sb("idx", [128, SC, NG], INT32)
        feat = sb("feat", [128, 2, GRP, S4, F])
        picked = sb("picked", [128, NO, SCB])
        tab_hi = sb("tab_hi", [KROWS, NO, KT, D], FP32R)
        tab_lo = sb("tab_lo", [KROWS, NO, KT, D], FP32R)
        ids_bc = sb("ids_bc", [KROWS, NO, SCB], INT32)
        onehot = sb("onehot", [KROWS, RING, SCB], FP32R)
        row_int = sb("row_int", [KROWS, KT], INT32)
        row_no = sb("row_no", [KROWS, KT])
        gram = sb("gram", [S4 * F, S4 * F, GRP])
        pairs = sb("pairs", [PAIRS, 2, NP3, TILE])
        dense = sb("dense", [128, BATCH])
        wd = feat[:, 1].rearrange("p g s f -> p (g s f)")[:, 0:2 * HID1].rearrange("p (h n) -> p h n", h=2)
        wds = sb("wds", [128, HID1])
        wp = sb("wp", [PAIRS, NP3, HID1])
        w2s = sb("w2s", [128, HID1 // 128, HID2])
        w3s = sb("w3s", [128, HID2 // 128])
        b1s = sb("b1s", [128, HID1 // 128])
        b2s = sb("b2s", [128, HID2 // 128])
        h1 = sb("h1", [128, HID1 // 128, TILE])
        h2 = sb("h2", [128, HID2 // 128, TILE])
        y = sb("y", [1, BATCH])
        ident = sb("ident", [128, 128])
        scratch = [nc.dram_tensor(f"gram_scratch{p}", [S4, (F + 1) * JEXT * GRP], FP32, kind="Internal").ap()
                   for p in range(2)]

        ps_tr = ps("ps_tr", [128, 2, 512])
        ps_gr = ps("ps_gr", [128, 2, 512])
        ps_oh = ps("ps_oh", [128, 2, 512])
        ps_l1 = ps("ps_l1", [128, 512])
        ps_l2 = ps("ps_l2", [128, 512])

        idx_in = sem("idx_in")
        tile_begun = sem("tile_begun")
        idx_set = sem("idx_set")
        rows_in = [sem(f"rows_in{t}") for t in range(SC)]
        tab_in = [sem(f"tab_in{n}") for n in range(4)]
        tab_h = sem("tab_h")
        tab_l = sem("tab_l")
        ids_in = sem("ids_in")
        w_in = sem("w_in")
        dense_in = sem("dense_in")
        rowno_i = sem("rowno_i")
        rowno_f = sem("rowno_f")
        ident0 = sem("ident0")
        ident1 = sem("ident1")
        wds_ok = sem("wds_ok")
        oh_set = sem("oh_set")
        oh_used = sem("oh_used")
        pick_sb = sem("pick_sb")
        tr_ps = sem("tr_ps")
        tr_sb = [sem("tr_sb_act"), sem("tr_sb_dve")]
        side = sem("side")
        gr_ps = sem("gr_ps")
        gr_sb = [sem("gr_sb_act"), sem("gr_sb_dve")]
        scr_in = sem("scr_in")
        pairs_in = [sem("pairs_in0"), sem("pairs_in1")]
        l1_ps = sem("l1_ps")
        l1_sb = sem("l1_sb")
        l2_ps = sem("l2_ps")
        l2_sb = sem("l2_sb")
        l3_ps = sem("l3_ps")
        y_sb = sem("y_sb")
        y_out = sem("y_out")

        W_IN = 16 * 6
        SCRW = 16 * 2 * S4
        PRW = 16 * NP3 * S4

        def fills(par, n):
            return (n + 1 - par) // 2

        def tr_copy(t, j):
            n = min(TRF, NG - TRF * j)
            f0 = 1 + TRF * j
            return (feat[:, t % 2, :, :, f0:f0 + n].rearrange("d g s f -> d f s g"),
                    ps_tr[:, (NTR * t + j) % 2, 0:n * TILE].rearrange("d (f s g) -> d f s g", f=n, s=S4))

        def gr_copy(q):
            return (gram[:, :, GPB * q:GPB * q + GPB],
                    ps_gr[0:S4 * F, q % 2, 0:GPB * S4 * F].rearrange("p (g c) -> p c g", g=GPB))

        block = ctx.enter_context(nc.Block())

        @block.sync
        def _(sp):
            def load_ids(k):
                sp.dma_start(ids_bc[:], ids_onehot[:, bass.ds(k * SCB, SCB)].unsqueeze(0)
                             .to_broadcast([KROWS, NO, SCB])).then_inc(ids_in, 16)

            sp.dma_start(idx_all[:], idx_rows).then_inc(idx_in, 16)
            load_ids(0)
            for n in range(NO):
                if n >= 4:
                    sp.wait_ge(tab_l, n - 3)
                sp.dma_start(rows[0:KROWS, 2 + n % 2, 8 * (n // 2 % 2):8 * (n // 2 % 2) + 8, :],
                             tables[ONEHOT[n]].rearrange("(p k) d -> p k d", k=KT)).then_inc(tab_in[n % 4], 16)
            sp.dma_start(dense[:], dense_t).then_inc(dense_in, 16)

            def superchunk(k, first, last):
                for t in range(SC):
                    tile = SC * k + t
                    n_gram = sp.compute_val(NGR // 2 * (tile + 1))
                    n_back = sp.compute_val(PRW * (2 * k + t // 2))
                    n_scratch = sp.compute_val(SCRW * (tile + 1))
                    n_layer1 = None if first and t < 2 else sp.compute_val(tile - 1)
                    if t == SC - 1 and not last:
                        sp.wait_ge(oh_set, NO * KT * (k + 1))
                        load_ids(k + 1)
                    sp.wait_ge(gr_sb[0], n_gram)
                    sp.wait_ge(gr_sb[1], n_gram)
                    if not (first and t < 2):
                        sp.wait_ge(l1_ps, n_layer1)
                        sp.wait_ge(pairs_in[t % 2], n_back)
                    for s in range(S4):
                        block_s = gram[F * s:F * s + F, F * s:F * s + F, :]
                        to = scratch[t % 2][s, 0:F * JEXT * GRP].rearrange("(i j g) -> i j g", i=F, j=JEXT)
                        sp.dma_start(to[:, 0:F, :], block_s).then_inc(scr_in, 16)
                        sp.dma_start(to[F - HALF:F, F:JEXT, :],
                                     gram[F * s + F - HALF:F * s + F, F * s:F * s + HALF, :]).then_inc(scr_in, 16)
                    sp.wait_ge(scr_in, n_scratch)
                    for a in range(NP3):
                        for s in range(S4):
                            at = (a * PI * (JEXT + 1) + 1) * GRP
                            skew = scratch[t % 2][s, at:at + PI * (JEXT + 1) * GRP].rearrange(
                                "(i k g) -> i k g", i=PI, k=JEXT + 1)[:, 0:HALF, :]
                            sp.dma_start(pairs[:, t % 2, a, GRP * s:GRP * s + GRP], skew).then_inc(pairs_in[t % 2], 16)

            superchunk(0, True, False)
            with sp.Fori(1, SUPERS - 1) as k:
                superchunk(k, False, False)
            superchunk(SUPERS - 1, False, True)
            sp.wait_ge(y_sb, TILES)
            sp.dma_start(out.rearrange("b o -> o b"), y[:]).then_inc(y_out, 16)
            sp.wait_ge(y_out, 16)

        @block.gpsimd
        def _(pool):
            def superchunk(k, first):
                for t in range(SC):
                    tile = SC * k + t
                    if not first:
                        pool.wait_ge(tr_ps, NTR * (tile - SC + 1))
                    nc.gpsimd.tensor_copy(idx[:, t, :], idx_all[:, bass.ds(tile * NG, NG)]).then_inc(idx_set, 1)
                    pool.wait_ge(idx_set, tile + 1)
                    pool.sem_inc(tile_begun, 1)
                    if first and t == 2:
                        pool.wait_ge(tab_l, NO)
                    for n, f in enumerate(GATHERED):
                        pool.indirect_dma_start(
                            out=rows[:, t, n, :], out_offset=None, in_=tables[f],
                            in_offset=bass.IndirectOffsetOnAxis(ap=idx[:, t, n:n + 1].bitcast(UINT32), axis=0),
                        ).then_inc(rows_in[t], 16)

            nc.gpsimd.iota(row_int[:], pattern=[[1, KT]], base=0, channel_multiplier=KT).then_inc(rowno_i, 1)
            nc.gpsimd.memset(ident[:], 0.0).then_inc(ident0, 1)
            pool.wait_ge(ident0, 1)
            nc.gpsimd.affine_select(out=ident[:], in_=ident[:], compare_op=ALU.not_equal, fill=1.0, base=0,
                                    pattern=[[-1, 128]], channel_multiplier=1).then_inc(ident1, 1)
            pool.wait_ge(idx_in, 16)
            superchunk(0, True)
            with pool.Fori(1, SUPERS) as k:
                superchunk(k, False)

        @block.scalar
        def _(act):
            act.dma_start(wd, w_dense.rearrange("(h p) n -> p h n", h=2)).then_inc(w_in, 16)
            act.dma_start(wp[:], w_pairs.rearrange("(a p) n -> p a n", a=NP3)).then_inc(w_in, 16)
            act.dma_start(w2s[:], w2.rearrange("(c p) n -> p c n", p=128)).then_inc(w_in, 16)
            with nc.allow_non_contiguous_dma(reason="a few columns"):
                act.dma_start(w3s[:], w3.rearrange("(c p) o -> p (c o)", p=128)).then_inc(w_in, 16)
                act.dma_start(b1s[:], b1.rearrange("(c p) -> p c", p=128)).then_inc(w_in, 16)
                act.dma_start(b2s[:], b2.rearrange("(c p) -> p c", p=128)).then_inc(w_in, 16)
            for n in range(NO):
                act.wait_ge(tab_in[n % 4], 16 * (n // 4 + 1))
                act.copy(tab_hi[:, n], rows[0:KROWS, 2 + n % 2, 8 * (n // 2 % 2):8 * (n // 2 % 2) + 8, :]).then_inc(tab_h, 1)

            act.wait_ge(w_in, W_IN)

            def pick_out(k, first):
                for n in range(NO):
                    act.wait_ge(oh_used, KT * (NO * k + n + 1))
                    if n == 0 and not first:
                        act.wait_ge(side, 2 * SC * k)
                    act.copy(picked[:, n, :], ps_oh[:, n % 2, :]).then_inc(pick_sb, 1)

            def relu1(tile):
                for c in range(HID1 // 128):
                    if c == 0:
                        act.wait_ge(l1_ps, tile + 1)
                    act.activation(h1[:, c, :], ps_l1[:, c * TILE:(c + 1) * TILE], ACT.Relu,
                                   bias=b1s[:, c:c + 1]).then_inc(l1_sb, 1)

            def superchunk(k, first):
                pick_out(k, first)
                for t in range(SC):
                    tile = SC * k + t
                    if first and t == 1:
                        act.wait_ge(wds_ok, 1)
                    for j in range(NTR):
                        if (NTR * t + j) % 2 == 0:
                            if j < 2 and not (first and t < 2):
                                act.wait_ge(gr_ps, NGR * (tile - 1))
                            act.wait_ge(tr_ps, NTR * tile + j + 1)
                            act.copy(*tr_copy(t, j)).then_inc(tr_sb[0], 1)
                    for q in range(0, NGR, 2):
                        if q == 0:
                            act.wait_ge(scr_in, SCRW * tile)
                        act.wait_ge(gr_ps, NGR * tile + q + 1)
                        act.copy(*gr_copy(q)).then_inc(gr_sb[0], 1)
                        if q == NGR - 4 and not (first and t < 2):
                            relu1(tile - 2)

            superchunk(0, True)
            with act.Fori(1, SUPERS) as k:
                superchunk(k, False)
            relu1(TILES - 2)
            relu1(TILES - 1)

        @block.vector
        def _(dve):
            dve.wait_ge(rowno_i, 1)
            nc.vector.tensor_copy(row_no[:], row_int[:]).then_inc(rowno_f, 1)
            dve.wait_ge(rowno_f, 1)
            for n in range(NO):
                dve.wait_ge(tab_h, n + 1)
                nc.vector.tensor_tensor(tab_lo[:, n], rows[0:KROWS, 2 + n % 2, 8 * (n // 2 % 2):8 * (n // 2 % 2) + 8, :],
                                        tab_hi[:, n].bitcast(FP32), ALU.subtract).then_inc(tab_l, 1)

            def make_onehots(k, first):
                dve.wait_ge(ids_in, 16 * (k + 1))
                for n in range(NO):
                    for kt in range(KT):
                        m = n * KT + kt
                        if not (first and m < RING):
                            dve.wait_ge(oh_used, NO * KT * k + m + 1 - RING)
                        nc.vector.tensor_scalar(onehot[:, m % RING, :], ids_bc[:, n, :], row_no[:, kt:kt + 1], None,
                                                ALU.is_equal).then_inc(oh_set, 1)

            def relu2(tile):
                for c in range(HID2 // 128):
                    if c == 0:
                        dve.wait_ge(l2_ps, tile + 1)
                    nc.vector.tensor_scalar(h2[:, c, :], ps_l2[:, c * TILE:(c + 1) * TILE], b2s[:, c:c + 1], 0.0,
                                            ALU.add, ALU.max).then_inc(l2_sb, 1)

            def take_y(tile):
                dve.wait_ge(l3_ps, tile + 1)
                nc.vector.tensor_copy(y[:, bass.ds(tile * TILE, TILE)],
                                      ps_l2[0:1, HID2:HID2 + TILE]).then_inc(y_sb, 1)

            def superchunk(k, first):
                make_onehots(k, first)
                if first:
                    dve.wait_ge(w_in, W_IN)
                    nc.vector.tensor_tensor(wds[:], wd[:, 0], wd[:, 1], ALU.add).then_inc(wds_ok, 1)
                    dve.wait_ge(dense_in, 16)
                for t in range(SC):
                    tile = SC * k + t
                    if not (first and t < 2):
                        dve.wait_ge(gr_ps, NGR * (tile - 1))
                    nc.vector.tensor_copy(feat[:, t % 2, :, :, 0].rearrange("d g s -> d s g"),
                                          dense[:, bass.ds(tile * TILE, TILE)].rearrange("d (s g) -> d s g", s=S4)
                                          ).then_inc(side, 1)
                    if t == 0:
                        dve.wait_ge(pick_sb, NO * (k + 1))
                    nc.vector.tensor_copy(feat[:, t % 2, :, :, 1 + NG:F].rearrange("d g s f -> d f s g"),
                                          picked[:, :, t * TILE:(t + 1) * TILE].rearrange("d f (s g) -> d f s g", s=S4)
                                          ).then_inc(side, 1)
                    for j in range(NTR):
                        if (NTR * t + j) % 2 == 1:
                            dve.wait_ge(tr_ps, NTR * tile + j + 1)
                            nc.vector.tensor_copy(*tr_copy(t, j)).then_inc(tr_sb[1], 1)
                    for q in range(1, NGR, 2):
                        if q == 1:
                            dve.wait_ge(scr_in, SCRW * tile)
                        if q == NGR - 1 and not (first and t < 2):
                            relu2(tile - 2)
                        dve.wait_ge(gr_ps, NGR * tile + q + 1)
                        nc.vector.tensor_copy(*gr_copy(q)).then_inc(gr_sb[1], 1)
                    if not (first and t < 2):
                        take_y(tile - 2)

            superchunk(0, True)
            with dve.Fori(1, SUPERS) as k:
                superchunk(k, False)
            for tile in range(TILES - 2, TILES):
                relu2(tile)
                take_y(tile)

        @block.tensor
        def _(pe):
            def pick(k, first):
                for n in range(NO):
                    if first and n < 2:
                        pass
                    elif n < 2:
                        pe.wait_ge(pick_sb, NO * k)
                    else:
                        pe.wait_ge(pick_sb, NO * k + n - 1)
                    if first:
                        pe.wait_ge(tab_l, n + 1)
                    for kt in range(KT):
                        m = n * KT + kt
                        pe.wait_ge(oh_set, NO * KT * k + m + 1)
                        pe.matmul(ps_oh[:, n % 2, :], tab_hi[:, n, kt, :], onehot[:, m % RING, :],
                                  start=(kt == 0), stop=False)
                        last = pe.matmul(ps_oh[:, n % 2, :], tab_lo[:, n, kt, :], onehot[:, m % RING, :],
                                         start=False, stop=(kt == KT - 1))
                        last.then_inc(oh_used, 1)

            def layer1(tile, par, n_par):
                pe.wait_ge(pairs_in[par], PRW * n_par)
                for c in range(HID1 // 128):
                    cols = slice(c * 128, (c + 1) * 128)
                    to = ps_l1[:, cols]
                    pe.matmul(to, wds[:, cols], dense[:, bass.ds(tile * TILE, TILE)], start=True, stop=False)
                    for a in range(NP3):
                        last = pe.matmul(to, wp[:, a, cols], pairs[:, par, a, :], start=False, stop=(a == NP3 - 1))
                last.then_inc(l1_ps, 1)

            def layer2(tile):
                pe.wait_ge(l1_sb, HID1 // 128 * (tile + 1))
                for m in range(HID2 // 128):
                    for c in range(HID1 // 128):
                        last = pe.matmul(ps_l2[:, m * TILE:(m + 1) * TILE], w2s[:, c, m * 128:(m + 1) * 128], h1[:, c, :],
                                         start=(c == 0), stop=(c == HID1 // 128 - 1))
                last.then_inc(l2_ps, 1)

            def layer3(tile):
                pe.wait_ge(l2_sb, HID2 // 128 * (tile + 1))
                for m in range(HID2 // 128):
                    last = pe.matmul(ps_l2[0:1, HID2:HID2 + TILE], w3s[:, m:m + 1], h2[:, m, :],
                                     start=(m == 0), stop=(m == HID2 // 128 - 1))
                last.then_inc(l3_ps, 1)

            def superchunk(k, first):
                pick(k, first)
                for t in range(SC):
                    tile = SC * k + t
                    mlp = not (first and t < 2)
                    pe.wait_ge(rows_in[t], 16 * NG * (k + 1))
                    for j in range(NTR):
                        n = NTR * t + j
                        if not (first and n < 2):
                            pe.wait_ge(tr_sb[n % 2], (NTR * SC // 2) * k + fills(n % 2, n))
                        for i in range(min(TRF, NG - TRF * j)):
                            last = pe.transpose(ps_tr[:, n % 2, i * TILE:(i + 1) * TILE],
                                                rows[:, t, TRF * j + i, :], ident[:])
                        last.then_inc(tr_ps, 1)
                    done = NTR * (t + 1)
                    pe.wait_ge(tr_sb[0], (NTR * SC // 2) * k + fills(0, done))
                    pe.wait_ge(tr_sb[1], (NTR * SC // 2) * k + fills(1, done))
                    pe.wait_ge(side, 2 * (tile + 1))
                    for q in range(NGR):
                        if not (first and t == 0 and q < 2):
                            pe.wait_ge(gr_sb[q % 2], NGR // 2 * tile + q // 2)
                        for i in range(GPB):
                            g = q * GPB + i
                            four = feat[:, t % 2, g].rearrange("d s f -> d (s f)")
                            last = pe.matmul(ps_gr[0:S4 * F, q % 2, i * S4 * F:(i + 1) * S4 * F], four, four,
                                             start=True, stop=True)
                        last.then_inc(gr_ps, 1)
                        if mlp and q == NGR - 3:
                            if first and t == 2:
                                pe.wait_ge(w_in, W_IN)
                                pe.wait_ge(wds_ok, 1)
                            else:
                                pe.wait_ge(l1_sb, HID1 // 128 * (tile - 2))
                            layer1(tile - 2, t % 2, 2 * k + t // 2)
                        if mlp and q == NGR - 2:
                            if not (first and t == 2):
                                pe.wait_ge(y_sb, tile - 2)
                            layer2(tile - 2)
                        if mlp and q == NGR - 1:
                            layer3(tile - 2)

            pe.wait_ge(ident1, 1)
            superchunk(0, True)
            with pe.Fori(1, SUPERS) as k:
                superchunk(k, False)
            for tile in range(TILES - 2, TILES):
                pe.wait_ge(l1_sb, HID1 // 128 * tile)
                layer1(tile, tile % 2, tile // 2 + 1)
                pe.wait_ge(y_sb, tile)
                layer2(tile)
                layer3(tile)


def kernel(**inputs):
    import concourse.bacc as bacc
    from concourse.bass_utils import run_bass_kernel_spmd

    a = {n: np.asarray(v) for n, v in inputs.items()}
    pair_row = np.zeros((F, F), np.int64)
    i0, i1 = np.triu_indices(F, k=1)
    pair_row[i0, i1] = D + np.arange(len(i0))
    order = []
    for i in range(F):
        for k in range(1, HALF + 1):
            i_ref, j_ref = ORDER[i], ORDER[(i + k) % F]
            order.append(pair_row[min(i_ref, j_ref), max(i_ref, j_ref)])
    w1 = a["W_top1"]
    n_pairs = len(order)
    arrays = {
        "dense_t": a["r_dense_features"].T,
        "idx_rows": a["ids"][:, GATHERED].reshape(TILES, TILE, NG).transpose(1, 0, 2).reshape(TILE, TILES * NG),
        "ids_onehot": a["ids"][:, ONEHOT].T,
        "w_dense": np.concatenate([w1[:D], w1[D + n_pairs:]]),
        "w_pairs": w1[np.array(order)],
        "b1": a["b_top1"], "w2": a["W_top2"], "b2": a["b_top2"], "w3": a["W_top3"],
    }
    arrays.update({f"tbl_{f}": a[f"tbl_{f}"] for f in range(N_TABLES)})
    arrays = {n: np.ascontiguousarray(v) for n, v in arrays.items()}

    nc = bacc.Bacc("TRN2", target_bir_lowering=False, num_devices=1)
    ap = {n: nc.dram_tensor(n, v.shape, mybir.dt.from_np(v.dtype), kind="ExternalInput").ap() for n, v in arrays.items()}
    out = nc.dram_tensor("y_out", (BATCH, 1), FP32, kind="ExternalOutput").ap()
    dlrm_tower(nc, ap["dense_t"], ap["idx_rows"], ap["ids_onehot"], [ap[f"tbl_{f}"] for f in range(N_TABLES)],
               ap["w_dense"], ap["w_pairs"], ap["b1"], ap["w2"], ap["b2"], ap["w3"], out)
    r = run_bass_kernel_spmd(nc, [arrays], core_ids=[0])
    return r.results[0]["y_out"]
```

```python
import numpy as np
import concourse.bass as bass
import concourse.mybir as mybir
from contextlib import ExitStack

FP32 = mybir.dt.float32
FP32R = mybir.dt.float32r
INT32 = mybir.dt.int32
UINT32 = mybir.dt.uint32
ALU = mybir.AluOpType
ACT = mybir.ActivationFunctionType

BATCH, D = 2048, 128
TABLE_ROWS = [12500, 125000, 1250, 12500, 12500, 12500, 1250, 12500, 1250, 12500, 1000, 1250, 12500,
              1250, 1000, 1250, 12500, 1000, 1000, 1000, 1000, 1250, 1250, 1250, 1000, 1000]
N_TABLES = len(TABLE_ROWS)
HID1, HID2 = 512, 256

ONEHOT_ROWS = 1000
ONEHOT = [f for f in range(N_TABLES) if TABLE_ROWS[f] == ONEHOT_ROWS][:7]
GATHERED = [f for f in range(N_TABLES) if f not in ONEHOT]
NO, NG = len(ONEHOT), len(GATHERED)
F = 1 + N_TABLES
ORDER = [0] + [1 + f for f in GATHERED] + [1 + f for f in ONEHOT]

TILE = 128
TILES = BATCH // TILE
SC = 4
SUPERS = TILES // SC
SCB = SC * TILE
S4 = 4
GRP = TILE // S4
KROWS = 125
KT = ONEHOT_ROWS // KROWS
HALF = F // 2
JEXT = 2 * F
PI = 9
NP3 = F // PI
PAIRS = PI * HALF

TRF = 4
NTR = -(-NG // TRF)
Q_L1, Q_L2, Q_L3 = 3, 5, 7
GPB = 4
NGR = GRP // GPB
BATCH_OH = 2
RING = 3
BATCHES = KT // BATCH_OH


def dlrm_tower(nc, dense_t, idx_rows, ids_onehot, tables, w_dense, w_pairs, b1, w2, b2, w3, out):
    ctx = ExitStack()
    with ctx:
        def sb(name, shape, dt=FP32):
            return ctx.enter_context(nc.sbuf_tensor(name, shape, dt))

        def ps(name, shape):
            return ctx.enter_context(nc.psum_tensor(name, shape, FP32))

        def sem(name):
            return ctx.enter_context(nc.semaphore(name))

        rows = sb("rows", [128, SC, NG, D])
        idx_all = sb("idx_all", [128, TILES * NG], INT32)
        idx = sb("idx", [128, SC, NG], INT32)
        feat = sb("feat", [128, 2, GRP, S4, F])
        picked = sb("picked", [128, NO, SCB])
        tab_hi = sb("tab_hi", [KROWS, NO, KT, D], FP32R)
        tab_lo = sb("tab_lo", [KROWS, NO, KT, D], FP32R)
        ids_bc = sb("ids_bc", [KROWS, 2, SCB], INT32)
        onehot = sb("onehot", [KROWS, RING * BATCH_OH, SCB], FP32R)
        row_int = sb("row_int", [KROWS, KT], INT32)
        row_no = sb("row_no", [KROWS, KT])
        gram = sb("gram", [S4 * F, 2, S4 * F, GRP])
        pairs = sb("pairs", [PAIRS, 2, NP3, TILE])
        dense = sb("dense", [128, BATCH])
        wd = feat[:, 1].rearrange("p g s f -> p (g s f)")[:, 0:2 * HID1].rearrange("p (h n) -> p h n", h=2)
        wds = sb("wds", [128, HID1])
        wp = sb("wp", [PAIRS, NP3, HID1])
        w2s = sb("w2s", [128, HID1 // 128, HID2])
        w3s = sb("w3s", [128, HID2 // 128])
        b1s = sb("b1s", [128, HID1 // 128])
        b2s = sb("b2s", [128, HID2 // 128])
        h1 = sb("h1", [128, HID1 // 128, TILE])
        h2 = sb("h2", [128, HID2 // 128, TILE])
        y = sb("y", [1, 2, TILE])
        ident = sb("ident", [128, 128])
        scratch = [nc.dram_tensor(f"gram_scratch{p}", [S4, (F + 1) * JEXT * GRP], FP32, kind="Internal").ap()
                   for p in range(2)]

        ps_tr = ps("ps_tr", [128, 2, 512])
        ps_gr = ps("ps_gr", [128, 2, 512])
        ps_oh = ps("ps_oh", [128, 2, 512])
        ps_l1 = ps("ps_l1", [128, 512])
        ps_l2 = ps("ps_l2", [128, 512])

        idx_in = sem("idx_in")
        tile_begun = sem("tile_begun")
        idx_set = sem("idx_set")
        rows_in = [sem(f"rows_in{t}") for t in range(SC)]
        tab_in = [sem(f"tab_in{n}") for n in range(4)]
        tab_h = sem("tab_h")
        tab_l = sem("tab_l")
        ids_in = [sem("ids_in0"), sem("ids_in1")]
        w_in = sem("w_in")
        dense_in = sem("dense_in")
        rowno_i = sem("rowno_i")
        rowno_f = sem("rowno_f")
        ident0 = sem("ident0")
        ident1 = sem("ident1")
        wds_ok = sem("wds_ok")
        oh_set = sem("oh_set")
        oh_used = sem("oh_used")
        pick_sb = sem("pick_sb")
        tr_ps = sem("tr_ps")
        tr_sb = [sem("tr_sb_act"), sem("tr_sb_dve")]
        side = sem("side")
        gr_ps = sem("gr_ps")
        gr_sb = [sem("gr_sb_act"), sem("gr_sb_dve")]
        scr_in = sem("scr_in")
        pairs_in = [sem("pairs_in0"), sem("pairs_in1")]
        l1_ps = sem("l1_ps")
        l1_sb = sem("l1_sb")
        l2_ps = sem("l2_ps")
        l2_sb = sem("l2_sb")
        l3_ps = sem("l3_ps")
        y_sb = sem("y_sb")
        y_out = [sem("y_out0"), sem("y_out1")]

        W_IN = 16 * 6
        SCRW = 16 * S4
        PRW = 16 * NP3 * S4

        def fills(par, n):
            return (n + 1 - par) // 2

        def tr_copy(t, j):
            n = min(TRF, NG - TRF * j)
            f0 = 1 + TRF * j
            return (feat[:, t % 2, :, :, f0:f0 + n].rearrange("d g s f -> d f s g"),
                    ps_tr[:, (NTR * t + j) % 2, 0:n * TILE].rearrange("d (f s g) -> d f s g", f=n, s=S4))

        def gr_copy(t, q):
            return (gram[:, t % 2, :, GPB * q:GPB * q + GPB],
                    ps_gr[0:S4 * F, q % 2, 0:GPB * S4 * F].rearrange("p (g c) -> p c g", g=GPB))

        block = ctx.enter_context(nc.Block())

        @block.sync
        def _(sp):
            sp.dma_start(idx_all[:], idx_rows).then_inc(idx_in, 16)
            for n in range(NO):
                if n >= 4:
                    sp.wait_ge(tab_l, n - 3)
                sp.dma_start(rows[0:KROWS, 2 + n % 2, 8 * (n // 2 % 2):8 * (n // 2 % 2) + 8, :],
                             tables[ONEHOT[n]].rearrange("(p k) d -> p k d", k=KT)).then_inc(tab_in[n % 4], 16)
            sp.dma_start(dense[:], dense_t).then_inc(dense_in, 16)

            def store_y(tile, par):
                sp.dma_start(out[bass.ds(tile * TILE, TILE), :].rearrange("b o -> o b"), y[:, par, :]).then_inc(y_out[par], 16)

            def superchunk(k, first):
                for t in range(SC):
                    tile = SC * k + t
                    n_gram = sp.compute_val(NGR // 2 * (tile + 1))
                    n_back = sp.compute_val(PRW * (2 * k + t // 2))
                    n_scratch = sp.compute_val(SCRW * (tile + 1))
                    n_layer1 = None if first and t < 2 else sp.compute_val(tile - 1)
                    sp.wait_ge(gr_sb[0], n_gram)
                    sp.wait_ge(gr_sb[1], n_gram)
                    if not (first and t < 2):
                        sp.wait_ge(l1_ps, n_layer1)
                        sp.wait_ge(pairs_in[t % 2], n_back)
                    for s in range(S4):
                        block_s = gram[F * s:F * s + F, t % 2, F * s:F * s + F, :].rearrange("i j g -> i (j g)")
                        to = scratch[t % 2][s, 0:F * JEXT * GRP].rearrange("(i r c) -> i r c", i=F, r=2)
                        sp.dma_start(to, block_s.unsqueeze(1).to_broadcast([F, 2, F * GRP])).then_inc(scr_in, 16)
                    sp.wait_ge(scr_in, n_scratch)
                    for a in range(NP3):
                        for s in range(S4):
                            at = (a * PI * (JEXT + 1) + 1) * GRP
                            skew = scratch[t % 2][s, at:at + PI * (JEXT + 1) * GRP].rearrange(
                                "(i k g) -> i k g", i=PI, k=JEXT + 1)[:, 0:HALF, :]
                            sp.dma_start(pairs[:, t % 2, a, GRP * s:GRP * s + GRP], skew).then_inc(pairs_in[t % 2], 16)
                    if not (first and t < 2):
                        sp.wait_ge(y_sb, n_layer1)
                        store_y(tile - 2, t % 2)

            superchunk(0, True)
            with sp.Fori(1, SUPERS) as k:
                superchunk(k, False)
            for tile in range(TILES - 2, TILES):
                sp.wait_ge(y_sb, tile + 1)
                store_y(tile, tile % 2)
            for par in range(2):
                sp.wait_ge(y_out[par], 16 * TILES // 2)

        @block.gpsimd
        def _(pool):
            def superchunk(k, first):
                for t in range(SC):
                    tile = SC * k + t
                    if not first:
                        pool.wait_ge(tr_ps, NTR * (tile - SC + 1))
                    nc.gpsimd.tensor_copy(idx[:, t, :], idx_all[:, bass.ds(tile * NG, NG)]).then_inc(idx_set, 1)
                    pool.wait_ge(idx_set, tile + 1)
                    pool.sem_inc(tile_begun, 1)
                    if first and t == 2:
                        pool.wait_ge(tab_l, NO)
                    for n, f in enumerate(GATHERED):
                        pool.indirect_dma_start(
                            out=rows[:, t, n, :], out_offset=None, in_=tables[f],
                            in_offset=bass.IndirectOffsetOnAxis(ap=idx[:, t, n:n + 1].bitcast(UINT32), axis=0),
                        ).then_inc(rows_in[t], 16)

            nc.gpsimd.iota(row_int[:], pattern=[[1, KT]], base=0, channel_multiplier=KT).then_inc(rowno_i, 1)
            nc.gpsimd.memset(ident[:], 0.0).then_inc(ident0, 1)
            pool.wait_ge(ident0, 1)
            nc.gpsimd.affine_select(out=ident[:], in_=ident[:], compare_op=ALU.not_equal, fill=1.0, base=0,
                                    pattern=[[-1, 128]], channel_multiplier=1).then_inc(ident1, 1)
            pool.wait_ge(idx_in, 16)
            superchunk(0, True)
            with pool.Fori(1, SUPERS) as k:
                superchunk(k, False)

        @block.scalar
        def _(act):
            def load_ids(k, n):
                act.dma_start(ids_bc[:, n % 2, :], ids_onehot[n, bass.ds(k * SCB, SCB)].unsqueeze(0)
                              .to_broadcast([KROWS, SCB])).then_inc(ids_in[n % 2], 16)

            load_ids(0, 0)
            load_ids(0, 1)
            def high_part(n):
                act.wait_ge(tab_in[n % 4], 16 * (n // 4 + 1))
                act.copy(tab_hi[:, n], rows[0:KROWS, 2 + n % 2, 8 * (n // 2 % 2):8 * (n // 2 % 2) + 8, :]).then_inc(tab_h, 1)

            def pick_out(k, first, n):
                act.wait_ge(oh_used, BATCHES * (NO * k + n + 1))
                if n == 0 and not first:
                    act.wait_ge(side, 2 * SC * k)
                act.copy(picked[:, n, :], ps_oh[:, n % 2, :]).then_inc(pick_sb, 1)

            def transposed(k, first, t, j):
                if (NTR * t + j) % 2 == 0:
                    if j < 2 and not (first and t < 2):
                        act.wait_ge(gr_ps, NGR * (SC * k + t - 1))
                    act.wait_ge(tr_ps, NTR * (SC * k + t) + j + 1)
                    act.copy(*tr_copy(t, j)).then_inc(tr_sb[0], 1)

            def relu1(tile):
                for c in range(HID1 // 128):
                    if c == 0:
                        act.wait_ge(l1_ps, tile + 1)
                    act.activation(h1[:, c, :], ps_l1[:, c * TILE:(c + 1) * TILE], ACT.Relu,
                                   bias=b1s[:, c:c + 1]).then_inc(l1_sb, 1)

            def superchunk(k, first, last):
                for n in range(NO):
                    if n + 2 < NO or not last:
                        act.wait_ge(oh_set, BATCHES * (NO * k + n + 1))
                        if n + 2 < NO:
                            load_ids(k, n + 2)
                        else:
                            load_ids(k + 1, n % 2)
                    pick_out(k, first, n)
                    if first and n + 4 < NO:
                        high_part(n + 4)
                    if not first and n >= NO - NTR:
                        transposed(k, first, 0, n - (NO - NTR))
                if first:
                    for j in range(NTR):
                        transposed(k, first, 0, j)
                    act.wait_ge(w_in, W_IN)
                    act.wait_ge(wds_ok, 1)
                for t in range(SC):
                    tile = SC * k + t
                    for q in range(NGR):
                        if q % 2 == 0:
                            if q == 0 and not (first and t < 2):
                                act.wait_ge(scr_in, SCRW * (tile - 1))
                            act.wait_ge(gr_ps, NGR * tile + q + 1)
                            act.copy(*gr_copy(t, q)).then_inc(gr_sb[0], 1)
                        if t < SC - 1 and q < NTR:
                            transposed(k, first, t + 1, q)
                        if q == Q_L1 and not (first and t < 2):
                            relu1(tile - 2)

            for n in range(4):
                high_part(n)
            act.dma_start(wd, w_dense.rearrange("(h p) n -> p h n", h=2)).then_inc(w_in, 16)
            act.dma_start(wp[:], w_pairs.rearrange("(a p) n -> p a n", a=NP3)).then_inc(w_in, 16)
            act.dma_start(w2s[:], w2.rearrange("(c p) n -> p c n", p=128)).then_inc(w_in, 16)
            with nc.allow_non_contiguous_dma(reason="a few columns"):
                act.dma_start(w3s[:], w3.rearrange("(c p) o -> p (c o)", p=128)).then_inc(w_in, 16)
                act.dma_start(b1s[:], b1.rearrange("(c p) -> p c", p=128)).then_inc(w_in, 16)
                act.dma_start(b2s[:], b2.rearrange("(c p) -> p c", p=128)).then_inc(w_in, 16)
            superchunk(0, True, False)
            with act.Fori(1, SUPERS - 1) as k:
                superchunk(k, False, False)
            superchunk(SUPERS - 1, False, True)
            relu1(TILES - 2)
            relu1(TILES - 1)

        @block.vector
        def _(dve):
            dve.wait_ge(rowno_i, 1)
            nc.vector.tensor_copy(row_no[:], row_int[:]).then_inc(rowno_f, 1)
            dve.wait_ge(rowno_f, 1)

            def split_table(n):
                dve.wait_ge(tab_h, n + 1)
                nc.vector.tensor_tensor(tab_lo[:, n], rows[0:KROWS, 2 + n % 2, 8 * (n // 2 % 2):8 * (n // 2 % 2) + 8, :],
                                        tab_hi[:, n].bitcast(FP32), ALU.subtract).then_inc(tab_l, 1)

            def make_onehots(k, first, n):
                dve.wait_ge(ids_in[n % 2], 16 * ((NO + 1 - n % 2) // 2 * k + n // 2 + 1))
                for h in range(BATCHES):
                    m = n * BATCHES + h
                    if m >= RING:
                        dve.wait_ge(oh_used, NO * BATCHES * k + m + 1 - RING)
                    elif not first:
                        dve.wait_ge(oh_used, NO * BATCHES * k)
                    for i in range(BATCH_OH):
                        kt = h * BATCH_OH + i
                        last = nc.vector.tensor_scalar(onehot[:, m % RING * BATCH_OH + i, :], ids_bc[:, n % 2, :],
                                                       row_no[:, kt:kt + 1], None, ALU.is_equal)
                    last.then_inc(oh_set, 1)

            def relu2(tile):
                for c in range(HID2 // 128):
                    if c == 0:
                        dve.wait_ge(l2_ps, tile + 1)
                    nc.vector.tensor_scalar(h2[:, c, :], ps_l2[:, c * TILE:(c + 1) * TILE], b2s[:, c:c + 1], 0.0,
                                            ALU.add, ALU.max).then_inc(l2_sb, 1)

            def take_y(tile, par):
                dve.wait_ge(l3_ps, tile + 1)
                nc.vector.tensor_copy(y[:, par, :], ps_l2[0:1, HID2:HID2 + TILE]).then_inc(y_sb, 1)

            def side_features(k, first, t):
                if not (first and t < 2):
                    dve.wait_ge(gr_ps, NGR * (SC * k + t - 1))
                nc.vector.tensor_copy(feat[:, t % 2, :, :, 0].rearrange("d g s -> d s g"),
                                      dense[:, bass.ds((SC * k + t) * TILE, TILE)].rearrange("d (s g) -> d s g", s=S4)
                                      ).then_inc(side, 1)
                if t == 0:
                    dve.wait_ge(pick_sb, NO * (k + 1))
                nc.vector.tensor_copy(feat[:, t % 2, :, :, 1 + NG:F].rearrange("d g s f -> d f s g"),
                                      picked[:, :, t * TILE:(t + 1) * TILE].rearrange("d f (s g) -> d f s g", s=S4)
                                      ).then_inc(side, 1)

            def transposed(k, first, t, j):
                if (NTR * t + j) % 2 == 1:
                    if j < 2 and not (first and t < 2):
                        dve.wait_ge(gr_ps, NGR * (SC * k + t - 1))
                    dve.wait_ge(tr_ps, NTR * (SC * k + t) + j + 1)
                    nc.vector.tensor_copy(*tr_copy(t, j)).then_inc(tr_sb[1], 1)

            def superchunk(k, first):
                for n in range(NO):
                    if first:
                        split_table(n)
                    make_onehots(k, first, n)
                    if not first and n >= NO - NTR:
                        transposed(k, first, 0, n - (NO - NTR))
                if first:
                    dve.wait_ge(w_in, W_IN)
                    nc.vector.tensor_tensor(wds[:], wd[:, 0], wd[:, 1], ALU.add).then_inc(wds_ok, 1)
                    for j in range(NTR):
                        transposed(k, first, 0, j)
                    dve.wait_ge(dense_in, 16)
                side_features(k, first, 0)
                for t in range(SC):
                    tile = SC * k + t
                    if t < SC - 1:
                        side_features(k, first, t + 1)
                    for q in range(NGR):
                        if q % 2 == 1:
                            if q == 1 and not (first and t < 2):
                                dve.wait_ge(scr_in, SCRW * (tile - 1))
                            dve.wait_ge(gr_ps, NGR * tile + q + 1)
                            nc.vector.tensor_copy(*gr_copy(t, q)).then_inc(gr_sb[1], 1)
                        if t < SC - 1 and q < NTR:
                            transposed(k, first, t + 1, q)
                        if q == Q_L2 and not (first and t < 2):
                            relu2(tile - 2)
                    if not (first and t < 2):
                        if not first:
                            dve.wait_ge(y_out[t % 2], 16 * (2 * k + t // 2 - 1))
                        take_y(tile - 2, t % 2)

            superchunk(0, True)
            with dve.Fori(1, SUPERS) as k:
                superchunk(k, False)
            for tile in range(TILES - 2, TILES):
                relu2(tile)
                dve.wait_ge(y_out[tile % 2], 16 * (tile // 2))
                take_y(tile, tile % 2)

        @block.tensor
        def _(pe):
            def pick(k, first, n):
                if n >= 2:
                    pe.wait_ge(pick_sb, NO * k + n - 1)
                elif not first:
                    pe.wait_ge(pick_sb, NO * k)
                if first:
                    pe.wait_ge(tab_l, n + 1)
                for h in range(BATCHES):
                    pe.wait_ge(oh_set, BATCHES * (NO * k + n) + h + 1)
                    for i in range(BATCH_OH):
                        kt, m = h * BATCH_OH + i, n * BATCHES + h
                        pe.matmul(ps_oh[:, n % 2, :], tab_hi[:, n, kt, :], onehot[:, m % RING * BATCH_OH + i, :],
                                  start=(kt == 0), stop=False)
                        last = pe.matmul(ps_oh[:, n % 2, :], tab_lo[:, n, kt, :], onehot[:, m % RING * BATCH_OH + i, :],
                                         start=False, stop=(kt == KT - 1))
                    last.then_inc(oh_used, 1)

            def transposes(k, first, t, j):
                if j == 0:
                    pe.wait_ge(rows_in[t], 16 * NG * (k + 1))
                n = NTR * t + j
                if not (first and n < 2):
                    pe.wait_ge(tr_sb[n % 2], (NTR * SC // 2) * k + fills(n % 2, n))
                for i in range(min(TRF, NG - TRF * j)):
                    last = pe.transpose(ps_tr[:, n % 2, i * TILE:(i + 1) * TILE], rows[:, t, TRF * j + i, :], ident[:])
                last.then_inc(tr_ps, 1)

            def interactions(k, first, t, q):
                tile = SC * k + t
                if q == 0:
                    done = NTR * (t + 1)
                    pe.wait_ge(tr_sb[0], (NTR * SC // 2) * k + fills(0, done))
                    pe.wait_ge(tr_sb[1], (NTR * SC // 2) * k + fills(1, done))
                    pe.wait_ge(side, 2 * (tile + 1))
                if not (first and t == 0 and q < 2):
                    pe.wait_ge(gr_sb[q % 2], NGR // 2 * tile + q // 2)
                for i in range(GPB):
                    four = feat[:, t % 2, q * GPB + i].rearrange("d s f -> d (s f)")
                    last = pe.matmul(ps_gr[0:S4 * F, q % 2, i * S4 * F:(i + 1) * S4 * F], four, four,
                                     start=True, stop=True)
                last.then_inc(gr_ps, 1)

            def layer1(tile, par, n_par):
                pe.wait_ge(pairs_in[par], PRW * n_par)
                for c in range(HID1 // 128):
                    cols = slice(c * 128, (c + 1) * 128)
                    to = ps_l1[:, cols]
                    pe.matmul(to, wds[:, cols], dense[:, bass.ds(tile * TILE, TILE)], start=True, stop=False)
                    for a in range(NP3):
                        last = pe.matmul(to, wp[:, a, cols], pairs[:, par, a, :], start=False, stop=(a == NP3 - 1))
                last.then_inc(l1_ps, 1)

            def layer2(tile):
                pe.wait_ge(l1_sb, HID1 // 128 * (tile + 1))
                for m in range(HID2 // 128):
                    for c in range(HID1 // 128):
                        last = pe.matmul(ps_l2[:, m * TILE:(m + 1) * TILE], w2s[:, c, m * 128:(m + 1) * 128], h1[:, c, :],
                                         start=(c == 0), stop=(c == HID1 // 128 - 1))
                last.then_inc(l2_ps, 1)

            def layer3(tile):
                pe.wait_ge(l2_sb, HID2 // 128 * (tile + 1))
                for m in range(HID2 // 128):
                    last = pe.matmul(ps_l2[0:1, HID2:HID2 + TILE], w3s[:, m:m + 1], h2[:, m, :],
                                     start=(m == 0), stop=(m == HID2 // 128 - 1))
                last.then_inc(l3_ps, 1)

            def superchunk(k, first):
                for n in range(NO):
                    pick(k, first, n)
                    if not first and n >= NO - NTR:
                        transposes(k, first, 0, n - (NO - NTR))
                if first:
                    for j in range(NTR):
                        transposes(k, first, 0, j)
                for t in range(SC):
                    tile = SC * k + t
                    mlp = not (first and t < 2)
                    for q in range(NGR):
                        interactions(k, first, t, q)
                        if t < SC - 1 and q < NTR:
                            transposes(k, first, t + 1, q)
                        if mlp and q == Q_L1:
                            if first and t == 2:
                                pe.wait_ge(w_in, W_IN)
                                pe.wait_ge(wds_ok, 1)
                            else:
                                pe.wait_ge(l1_sb, HID1 // 128 * (tile - 2))
                            layer1(tile - 2, t % 2, 2 * k + t // 2)
                        if mlp and q == Q_L2:
                            if not (first and t == 2):
                                pe.wait_ge(y_sb, tile - 2)
                            layer2(tile - 2)
                        if mlp and q == Q_L3:
                            layer3(tile - 2)

            pe.wait_ge(ident1, 1)
            superchunk(0, True)
            with pe.Fori(1, SUPERS) as k:
                superchunk(k, False)
            for tile in range(TILES - 2, TILES):
                pe.wait_ge(l1_sb, HID1 // 128 * tile)
                layer1(tile, tile % 2, tile // 2 + 1)
                pe.wait_ge(y_sb, tile)
                layer2(tile)
                layer3(tile)


def kernel(**inputs):
    import concourse.bacc as bacc
    from concourse.bass_utils import run_bass_kernel_spmd

    a = {n: np.asarray(v) for n, v in inputs.items()}
    pair_row = np.zeros((F, F), np.int64)
    i0, i1 = np.triu_indices(F, k=1)
    pair_row[i0, i1] = D + np.arange(len(i0))
    order = []
    for i in range(F):
        for k in range(1, HALF + 1):
            i_ref, j_ref = ORDER[i], ORDER[(i + k) % F]
            order.append(pair_row[min(i_ref, j_ref), max(i_ref, j_ref)])
    w1 = a["W_top1"]
    n_pairs = len(order)
    arrays = {
        "dense_t": a["r_dense_features"].T,
        "idx_rows": a["ids"][:, GATHERED].reshape(TILES, TILE, NG).transpose(1, 0, 2).reshape(TILE, TILES * NG),
        "ids_onehot": a["ids"][:, ONEHOT].T,
        "w_dense": np.concatenate([w1[:D], w1[D + n_pairs:]]),
        "w_pairs": w1[np.array(order)],
        "b1": a["b_top1"], "w2": a["W_top2"], "b2": a["b_top2"], "w3": a["W_top3"],
    }
    arrays.update({f"tbl_{f}": a[f"tbl_{f}"] for f in range(N_TABLES)})
    arrays = {n: np.ascontiguousarray(v) for n, v in arrays.items()}

    nc = bacc.Bacc("TRN2", target_bir_lowering=False, num_devices=1)
    ap = {n: nc.dram_tensor(n, v.shape, mybir.dt.from_np(v.dtype), kind="ExternalInput").ap() for n, v in arrays.items()}
    out = nc.dram_tensor("y_out", (BATCH, 1), FP32, kind="ExternalOutput").ap()
    dlrm_tower(nc, ap["dense_t"], ap["idx_rows"], ap["ids_onehot"], [ap[f"tbl_{f}"] for f in range(N_TABLES)],
               ap["w_dense"], ap["w_pairs"], ap["b1"], ap["w2"], ap["b2"], ap["w3"], out)
    r = run_bass_kernel_spmd(nc, [arrays], core_ids=[0])
    return r.results[0]["y_out"]
```

```python
import numpy as np
import concourse.bass as bass
import concourse.mybir as mybir
from contextlib import ExitStack

FP32 = mybir.dt.float32
FP32R = mybir.dt.float32r
INT32 = mybir.dt.int32
UINT32 = mybir.dt.uint32
ALU = mybir.AluOpType
ACT = mybir.ActivationFunctionType

BATCH, D = 2048, 128
TABLE_ROWS = [12500, 125000, 1250, 12500, 12500, 12500, 1250, 12500, 1250, 12500, 1000, 1250, 12500,
              1250, 1000, 1250, 12500, 1000, 1000, 1000, 1000, 1250, 1250, 1250, 1000, 1000]
N_TABLES = len(TABLE_ROWS)
HID1, HID2 = 512, 256

ONEHOT_ROWS = 1000
ONEHOT = [f for f in range(N_TABLES) if TABLE_ROWS[f] == ONEHOT_ROWS][:7]
GATHERED = [f for f in range(N_TABLES) if f not in ONEHOT]
NO, NG = len(ONEHOT), len(GATHERED)
F = 1 + N_TABLES
ORDER = [0] + [1 + f for f in GATHERED] + [1 + f for f in ONEHOT]

TILE = 128
TILES = BATCH // TILE
SC = 4
SUPERS = TILES // SC
SCB = SC * TILE
S4 = 4
GRP = TILE // S4
KROWS = 125
KT = ONEHOT_ROWS // KROWS
HALF = F // 2
JEXT = 2 * F
PI = 9
NP3 = F // PI
PAIRS = PI * HALF

TRF = 4
NTR = -(-NG // TRF)
Q_L1, Q_L2, Q_L3 = 3, 5, 7
GPB = 4
NGR = GRP // GPB
BATCH_OH = 2
RING = 3
BATCHES = KT // BATCH_OH
NB = NO * BATCHES
Q_TR = 3
U_MAKE, U_PICK = 2, 3
TR0_BEHIND = [min(2 + j, NO - 2) for j in range(NTR)]
assert U_PICK + NB < SC * NGR and Q_TR + NTR <= NGR


def dlrm_tower(nc, dense_t, idx_rows, ids_onehot, tables, w_dense, w_pairs, b1, w2, b2, w3, out):
    ctx = ExitStack()
    with ctx:
        def sb(name, shape, dt=FP32):
            return ctx.enter_context(nc.sbuf_tensor(name, shape, dt))

        def ps(name, shape):
            return ctx.enter_context(nc.psum_tensor(name, shape, FP32))

        def sem(name):
            return ctx.enter_context(nc.semaphore(name))

        rows = sb("rows", [128, 2, NG, D])
        idx_all = sb("idx_all", [128, TILES * NG], INT32)
        idx = sb("idx", [128, 2, NG], INT32)
        feat = sb("feat", [128, 2, GRP, S4, F])
        picked = sb("picked", [128, 2, NO, SCB])
        tab_hi = sb("tab_hi", [KROWS, NO, KT, D], FP32R)
        tab_lo = sb("tab_lo", [KROWS, NO, KT, D], FP32R)
        ids_bc = sb("ids_bc", [KROWS, 2, SCB], INT32)
        onehot = sb("onehot", [KROWS, RING * BATCH_OH, SCB], FP32R)
        row_int = sb("row_int", [KROWS, KT], INT32)
        row_no = sb("row_no", [KROWS, KT])
        gram = sb("gram", [S4 * F, 2, S4 * F, GRP])
        pairs = sb("pairs", [PAIRS, 2, NP3, TILE])
        dense = sb("dense", [128, BATCH])
        odd_feat = feat[:, 1].rearrange("p g s f -> p (g s f)")
        wd = odd_feat[:, 0:2 * HID1].rearrange("p (h n) -> p h n", h=2)
        odd_picks = picked[:, 1].rearrange("p n b -> p (n b)")
        IN_ROWS, IN_FEAT = 2, 2
        raw = []
        for n in range(NO):
            if n < IN_ROWS:
                raw.append(rows[0:KROWS, 1, KT * n:KT * (n + 1), :])
            elif n < IN_ROWS + IN_FEAT:
                at = 2 * HID1 + (n - IN_ROWS) * KT * D
                raw.append(odd_feat[0:KROWS, at:at + KT * D].rearrange("p (k d) -> p k d", k=KT))
            else:
                at = (n - IN_ROWS - IN_FEAT) * KT * D
                raw.append(odd_picks[0:KROWS, at:at + KT * D].rearrange("p (k d) -> p k d", k=KT))
        wds = sb("wds", [128, HID1])
        wp = sb("wp", [PAIRS, NP3, HID1])
        w2s = sb("w2s", [128, HID1 // 128, HID2])
        w3s = sb("w3s", [128, HID2 // 128])
        b1s = sb("b1s", [128, HID1 // 128])
        b2s = sb("b2s", [128, HID2 // 128])
        h1 = sb("h1", [128, HID1 // 128, TILE])
        h2 = sb("h2", [128, HID2 // 128, TILE])
        y = sb("y", [1, 2, TILE])
        ident = sb("ident", [128, 128])
        scratch = [nc.dram_tensor(f"gram_scratch{p}", [S4, (F + 1) * JEXT * GRP], FP32, kind="Internal").ap()
                   for p in range(2)]

        ps_tr = ps("ps_tr", [128, 2, 512])
        ps_gr = ps("ps_gr", [128, 2, 512])
        ps_oh = ps("ps_oh", [128, 2, 512])
        ps_l1 = ps("ps_l1", [128, 512])
        ps_l2 = ps("ps_l2", [128, 512])

        idx_in = sem("idx_in")
        tile_begun = sem("tile_begun")
        idx_set = sem("idx_set")
        rows_in = [[sem(f"rows_in{p}{j}") for j in range(NTR)] for p in range(2)]
        tab_in = [sem(f"tab_in{n}") for n in range(NO)]
        tab_h = sem("tab_h")
        tab_l = sem("tab_l")
        ids_in = [sem("ids_in0"), sem("ids_in1")]
        w_in = sem("w_in")
        dense_in = sem("dense_in")
        rowno_i = sem("rowno_i")
        rowno_f = sem("rowno_f")
        ident0 = sem("ident0")
        ident1 = sem("ident1")
        wds_ok = sem("wds_ok")
        oh_set = sem("oh_set")
        oh_used = sem("oh_used")
        pick_sb = sem("pick_sb")
        tr_ps = sem("tr_ps")
        tr_sb = [sem("tr_sb_act"), sem("tr_sb_dve")]
        side = sem("side")
        gr_ps = sem("gr_ps")
        gr_sb = [sem("gr_sb_act"), sem("gr_sb_dve")]
        scr_in = sem("scr_in")
        scr_in_pool = sem("scr_in_pool")
        pairs_in = [[sem(f"pairs_in{p}{a}") for a in range(NP3)] for p in range(2)]
        pairs_in_pool = sem("pairs_in_pool")
        l1_ps = sem("l1_ps")
        l1_sb = sem("l1_sb")
        l2_ps = sem("l2_ps")
        l2_sb = sem("l2_sb")
        l3_ps = sem("l3_ps")
        y_sb = sem("y_sb")
        y_out = [sem("y_out0"), sem("y_out1")]

        W_IN = 16 * 6
        SCRW = 16 * S4
        PRW = 16 * S4

        def fills(par, n):
            return (n + 1 - par) // 2

        def fill_size(j):
            return min(TRF, NG - TRF * j)

        def tr_copy(t, j):
            n = fill_size(j)
            f0 = 1 + TRF * j
            return (feat[:, t % 2, :, :, f0:f0 + n].rearrange("d g s f -> d f s g"),
                    ps_tr[:, (NTR * t + j) % 2, 0:n * TILE].rearrange("d (f s g) -> d f s g", f=n, s=S4))

        def gr_copy(t, q):
            return (gram[:, t % 2, :, GPB * q:GPB * q + GPB],
                    ps_gr[0:S4 * F, q % 2, 0:GPB * S4 * F].rearrange("p (g c) -> p c g", g=GPB))

        def write_scratch(queue, par, s, written):
            block_s = gram[F * s:F * s + F, par, F * s:F * s + F, :].rearrange("i j g -> i (j g)")
            to = scratch[par][s, 0:F * JEXT * GRP].rearrange("(i r c) -> i r c", i=F, r=2)
            queue.dma_start(to, block_s.unsqueeze(1).to_broadcast([F, 2, F * GRP])).then_inc(written, 16)

        def read_pairs(queue, par, a, read):
            at = (a * PI * (JEXT + 1) + 1) * GRP
            for s in range(S4):
                skew = scratch[par][s, at:at + PI * (JEXT + 1) * GRP].rearrange(
                    "(i k g) -> i k g", i=PI, k=JEXT + 1)[:, 0:HALF, :]
                queue.dma_start(pairs[:, par, a, GRP * s:GRP * s + GRP], skew).then_inc(read, 16)

        block = ctx.enter_context(nc.Block())

        @block.sync
        def _(sp):
            sp.dma_start(idx_all[:], idx_rows).then_inc(idx_in, 16)
            for n in range(NO):
                sp.dma_start(raw[n], tables[ONEHOT[n]].rearrange("(p k) d -> p k d", k=KT)).then_inc(tab_in[n], 16)
            sp.wait_ge(tab_in[NO - 1], 16)
            sp.dma_start(dense[:], dense_t).then_inc(dense_in, 16)

            def store_y(tile, par):
                sp.dma_start(out[bass.ds(tile * TILE, TILE), :].rearrange("b o -> o b"), y[:, par, :]).then_inc(y_out[par], 16)

            def round_trip(k, t, first, last_tile):
                tile = SC * k + t
                n_gram = sp.compute_val(NGR // 2 * (tile + 1))
                n_back = sp.compute_val(PRW * (2 * k + t // 2))
                n_scratch = sp.compute_val(SCRW * (tile + 1) - (16 if last_tile else 0))
                n_layer1 = None if first and t < 2 else sp.compute_val(tile - 1)
                sp.wait_ge(gr_sb[0], n_gram)
                sp.wait_ge(gr_sb[1], n_gram)
                if not (first and t < 2):
                    sp.wait_ge(l1_ps, n_layer1)
                    for a in range(NP3):
                        sp.wait_ge(pairs_in[t % 2][a], n_back)
                for s in range(S4 - 1 if last_tile else S4):
                    write_scratch(sp, t % 2, s, scr_in)
                sp.wait_ge(scr_in, n_scratch)
                if last_tile:
                    sp.wait_ge(scr_in_pool, 16)
                for a in range(NP3 - 1 if last_tile else NP3):
                    read_pairs(sp, t % 2, a, pairs_in[t % 2][a])
                if not (first and t < 2) and not last_tile:
                    sp.wait_ge(y_sb, n_layer1)
                    store_y(tile - 2, t % 2)

            for t in range(SC):
                round_trip(0, t, True, False)
            with sp.Fori(1, SUPERS - 1) as k:
                for t in range(SC):
                    round_trip(k, t, False, False)
            for t in range(SC):
                round_trip(SUPERS - 1, t, False, t == SC - 1)
            for tile in range(TILES - 3, TILES):
                sp.wait_ge(y_sb, tile + 1)
                store_y(tile, tile % 2)
            for par in range(2):
                sp.wait_ge(y_out[par], 16 * TILES // 2)

        @block.gpsimd
        def _(pool):
            def superchunk(k, first):
                for t in range(SC):
                    tile = SC * k + t
                    if not (first and t < 2):
                        pool.wait_ge(tr_ps, NTR * (tile - 1))
                    pool.wait_ge(idx_set, tile + 1)
                    pool.sem_inc(tile_begun, 1)
                    if first and t == 1:
                        pool.wait_ge(tab_l, IN_ROWS)
                    for n, f in enumerate(GATHERED):
                        pool.indirect_dma_start(
                            out=rows[:, t % 2, n, :], out_offset=None, in_=tables[f],
                            in_offset=bass.IndirectOffsetOnAxis(ap=idx[:, t % 2, n:n + 1].bitcast(UINT32), axis=0),
                        ).then_inc(rows_in[t % 2][n // TRF], 16)

            nc.gpsimd.iota(row_int[:], pattern=[[1, KT]], base=0, channel_multiplier=KT).then_inc(rowno_i, 1)
            nc.gpsimd.memset(ident[:], 0.0).then_inc(ident0, 1)
            pool.wait_ge(ident0, 1)
            nc.gpsimd.affine_select(out=ident[:], in_=ident[:], compare_op=ALU.not_equal, fill=1.0, base=0,
                                    pattern=[[-1, 128]], channel_multiplier=1).then_inc(ident1, 1)
            superchunk(0, True)
            with pool.Fori(1, SUPERS) as k:
                superchunk(k, False)

            par = (TILES - 1) % 2
            pool.wait_ge(gr_sb[0], NGR // 2 * TILES)
            pool.wait_ge(gr_sb[1], NGR // 2 * TILES)
            pool.wait_ge(l1_ps, TILES - 2)
            for a in range(NP3):
                pool.wait_ge(pairs_in[par][a], PRW * (TILES // 2 - 1))
            write_scratch(pool, par, S4 - 1, scr_in_pool)
            pool.wait_ge(scr_in, SCRW * TILES - 16)
            pool.wait_ge(scr_in_pool, 16)
            read_pairs(pool, par, NP3 - 1, pairs_in_pool)

        @block.scalar
        def _(act):
            def load_ids(k, n):
                act.dma_start(ids_bc[:, n % 2, :], ids_onehot[n, bass.ds(k * SCB, SCB)].unsqueeze(0)
                              .to_broadcast([KROWS, SCB])).then_inc(ids_in[n % 2], 16)

            def high_part(n):
                act.wait_ge(tab_in[n], 16)
                act.copy(tab_hi[:, n], raw[n]).then_inc(tab_h, 1)

            def next_ids(k, n):
                if n + 2 < NO:
                    act.wait_ge(oh_set, NB * k + BATCHES * (n + 1))
                    load_ids(k, n + 2)

            def pick_out(k, par, n, reused):
                act.wait_ge(oh_used, NB * k + BATCHES * (n + 1))
                if n == 0 and reused:
                    act.wait_ge(side, 2 * SC * (k - 1))
                act.copy(picked[:, par, n, :], ps_oh[:, n % 2, :]).then_inc(pick_sb, 1)

            def transposed(k, first, t, j):
                if (NTR * t + j) % 2 == 0:
                    if j < 2 and not (first and t < 2):
                        act.wait_ge(gr_ps, NGR * (SC * k + t - 1))
                    act.wait_ge(tr_ps, NTR * (SC * k + t) + j + 1)
                    act.copy(*tr_copy(t, j)).then_inc(tr_sb[0], 1)

            def relu1(tile):
                for c in range(HID1 // 128):
                    if c == 0:
                        act.wait_ge(l1_ps, tile + 1)
                    act.activation(h1[:, c, :], ps_l1[:, c * TILE:(c + 1) * TILE], ACT.Relu,
                                   bias=b1s[:, c:c + 1]).then_inc(l1_sb, 1)

            def superchunk(k, first, last):
                for t in range(SC):
                    tile = SC * k + t
                    for q in range(NGR):
                        u = NGR * t + q
                        if not last:
                            if u == 0:
                                act.wait_ge(oh_set, NB * (k + 1))
                                load_ids(k + 1, 0)
                                load_ids(k + 1, 1)
                            n, h = divmod(u - U_MAKE, BATCHES)
                            if h == 0 and 1 <= n <= NO:
                                next_ids(k + 1, n - 1)
                            n, h = divmod(u - U_PICK, BATCHES)
                            if h == 0 and 1 <= n <= NO:
                                pick_out(k + 1, 1 if first else (k + 1) % 2, n - 1, not first)
                        if q % 2 == 0:
                            if q == 0 and not (first and t < 2):
                                act.wait_ge(scr_in, SCRW * (tile - 1))
                            act.wait_ge(gr_ps, NGR * tile + q + 1)
                            act.copy(*gr_copy(t, q)).then_inc(gr_sb[0], 1)
                        if q == Q_L1 and not (first and t < 2) and not (last and t == SC - 1):
                            relu1(tile - 2)
                        if 0 <= q - Q_TR < NTR and not (last and t >= SC - 2):
                            transposed(k, first, t + 1, q - Q_TR)
                    if last and t == SC - 2:
                        relu1(tile - 1)
                        for j in range(NTR):
                            transposed(k, first, t + 1, j)

            load_ids(0, 0)
            load_ids(0, 1)
            for n in range(3):
                high_part(n)
            for n in range(NO):
                if n == NO - 2:
                    act.dma_start(wd, w_dense.rearrange("(h p) n -> p h n", h=2)).then_inc(w_in, 16)
                    act.dma_start(wp[:], w_pairs.rearrange("(a p) n -> p a n", a=NP3)).then_inc(w_in, 16)
                    act.dma_start(w2s[:], w2.rearrange("(c p) n -> p c n", p=128)).then_inc(w_in, 16)
                    with nc.allow_non_contiguous_dma(reason="a few columns"):
                        act.dma_start(w3s[:], w3.rearrange("(c p) o -> p (c o)", p=128)).then_inc(w_in, 16)
                        act.dma_start(b1s[:], b1.rearrange("(c p) -> p c", p=128)).then_inc(w_in, 16)
                        act.dma_start(b2s[:], b2.rearrange("(c p) -> p c", p=128)).then_inc(w_in, 16)
                next_ids(0, n)
                if n + 3 < NO:
                    high_part(n + 3)
                pick_out(0, 0, n, False)
                for j in range(NTR):
                    if TR0_BEHIND[j] == n:
                        transposed(0, True, 0, j)
            act.wait_ge(tab_l, NO)
            act.wait_ge(w_in, W_IN)
            act.wait_ge(wds_ok, 1)
            superchunk(0, True, False)
            with act.Fori(1, SUPERS - 1) as k:
                superchunk(k, False, False)
            superchunk(SUPERS - 1, False, True)
            for tile in range(TILES - 2, TILES):
                relu1(tile)

        @block.vector
        def _(dve):
            dve.wait_ge(rowno_i, 1)
            nc.vector.tensor_copy(row_no[:], row_int[:]).then_inc(rowno_f, 1)
            dve.wait_ge(rowno_f, 1)

            def set_idx(tile, par):
                nc.vector.tensor_copy(idx[:, par, :], idx_all[:, bass.ds(tile * NG, NG)]).then_inc(idx_set, 1)

            def split_table(n):
                dve.wait_ge(tab_h, n + 1)
                nc.vector.tensor_tensor(tab_lo[:, n], raw[n], tab_hi[:, n].bitcast(FP32),
                                        ALU.subtract).then_inc(tab_l, 1)

            def make_onehots(k, n, h, reused):
                if h == 0:
                    dve.wait_ge(ids_in[n % 2], 16 * ((NO + 1 - n % 2) // 2 * k + n // 2 + 1))
                m = n * BATCHES + h
                if m >= RING or reused:
                    dve.wait_ge(oh_used, NB * k + max(m + 1 - RING, 0))
                for i in range(BATCH_OH):
                    kt = h * BATCH_OH + i
                    made = nc.vector.tensor_scalar(onehot[:, m % RING * BATCH_OH + i, :], ids_bc[:, n % 2, :],
                                                   row_no[:, kt:kt + 1], None, ALU.is_equal)
                made.then_inc(oh_set, 1)

            def relu2(tile):
                for c in range(HID2 // 128):
                    if c == 0:
                        dve.wait_ge(l2_ps, tile + 1)
                    nc.vector.tensor_scalar(h2[:, c, :], ps_l2[:, c * TILE:(c + 1) * TILE], b2s[:, c:c + 1], 0.0,
                                            ALU.add, ALU.max).then_inc(l2_sb, 1)

            def take_y(tile, par, stored):
                if stored is not None:
                    dve.wait_ge(y_out[par], 16 * stored)
                dve.wait_ge(l3_ps, tile + 1)
                nc.vector.tensor_copy(y[:, par, :], ps_l2[0:1, HID2:HID2 + TILE]).then_inc(y_sb, 1)

            def whole_relu2(tile):
                relu2(tile)
                take_y(tile, tile % 2, tile // 2)

            def side_features(k, first, t):
                k_of, t_of = (k + 1, 0) if t == SC else (k, t)
                par = k_of if first else k_of % 2
                if not (first and t < 2):
                    dve.wait_ge(gr_ps, NGR * (SC * k + t - 1))
                nc.vector.tensor_copy(feat[:, t % 2, :, :, 0].rearrange("d g s -> d s g"),
                                      dense[:, bass.ds((SC * k + t) * TILE, TILE)].rearrange("d (s g) -> d s g", s=S4)
                                      ).then_inc(side, 1)
                if t_of == 0:
                    dve.wait_ge(pick_sb, NO * (k_of + 1))
                nc.vector.tensor_copy(feat[:, t % 2, :, :, 1 + NG:F].rearrange("d g s f -> d f s g"),
                                      picked[:, par, :, t_of * TILE:(t_of + 1) * TILE].rearrange(
                                          "d f (s g) -> d f s g", s=S4)).then_inc(side, 1)

            def transposed(k, first, t, j):
                if (NTR * t + j) % 2 == 1:
                    if j < 2 and not (first and t < 2):
                        dve.wait_ge(gr_ps, NGR * (SC * k + t - 1))
                    dve.wait_ge(tr_ps, NTR * (SC * k + t) + j + 1)
                    nc.vector.tensor_copy(*tr_copy(t, j)).then_inc(tr_sb[1], 1)

            def superchunk(k, first, last):
                for t in range(SC):
                    tile = SC * k + t
                    mlp = not (first and t < 2) and not (last and t == SC - 1)
                    if t < SC - 1:
                        side_features(k, first, t + 1)
                    for q in range(NGR):
                        m = NGR * t + q - U_MAKE
                        if not last and 0 <= m < NB:
                            make_onehots(k + 1, m // BATCHES, m % BATCHES, True)
                        if not last and t == SC - 1 and q == NGR - 1:
                            side_features(k, first, SC)
                        if q % 2 == 1:
                            if q == 1 and not (first and t < 2):
                                dve.wait_ge(scr_in, SCRW * (tile - 1))
                            dve.wait_ge(gr_ps, NGR * tile + q + 1)
                            nc.vector.tensor_copy(*gr_copy(t, q)).then_inc(gr_sb[1], 1)
                        if q == Q_TR and not (last and t > 0):
                            for j in range(NTR):
                                dve.wait_ge(rows_in[(t + 1) % 2][j], 16 * fill_size(j) * (2 * k + (t + 1) // 2 + 1))
                            set_idx(tile + 3, (t + 1) % 2)
                        if 0 <= q - Q_TR < NTR and not (last and t >= SC - 2):
                            transposed(k, first, t + 1, q - Q_TR)
                        if mlp and q == Q_L2:
                            relu2(tile - 2)
                    if mlp:
                        take_y(tile - 2, t % 2, None if first else 2 * k + t // 2 - 1)
                    if last and t == SC - 2:
                        for j in range(NTR):
                            transposed(k, first, t + 1, j)

            dve.wait_ge(idx_in, 16)
            set_idx(0, 0)
            set_idx(1, 1)
            for n in range(NO):
                split_table(n)
                for h in range(BATCHES):
                    if h == RING - 1:
                        for j in range(NTR):
                            if TR0_BEHIND[j] == n - 1:
                                transposed(0, True, 0, j)
                    make_onehots(0, n, h, False)
                if n == NO // 2:
                    for j in range(NTR):
                        dve.wait_ge(rows_in[0][j], 16 * fill_size(j))
                    set_idx(2, 0)
            dve.wait_ge(w_in, W_IN)
            nc.vector.tensor_tensor(wds[:], wd[:, 0], wd[:, 1], ALU.add).then_inc(wds_ok, 1)
            dve.wait_ge(dense_in, 16)
            dve.wait_ge(tab_l, NO)
            dve.wait_ge(wds_ok, 1)
            side_features(0, True, 0)
            superchunk(0, True, False)
            with dve.Fori(1, SUPERS - 1) as k:
                superchunk(k, False, False)
            superchunk(SUPERS - 1, False, True)
            for tile in range(TILES - 3, TILES):
                whole_relu2(tile)

        @block.tensor
        def _(pe):
            def pick(k, n, h, reused):
                if h == 0:
                    if n >= 2 or reused:
                        pe.wait_ge(pick_sb, NO * k + max(n - 1, 0))
                    if not reused:
                        pe.wait_ge(tab_l, n + 1)
                m = n * BATCHES + h
                pe.wait_ge(oh_set, NB * k + m + 1)
                for i in range(BATCH_OH):
                    kt = h * BATCH_OH + i
                    one = onehot[:, m % RING * BATCH_OH + i, :]
                    pe.matmul(ps_oh[:, n % 2, :], tab_hi[:, n, kt, :], one, start=(kt == 0), stop=False)
                    done = pe.matmul(ps_oh[:, n % 2, :], tab_lo[:, n, kt, :], one, start=False, stop=(kt == KT - 1))
                done.then_inc(oh_used, 1)

            def transposes(k, first, t, j):
                pe.wait_ge(rows_in[t % 2][j], 16 * fill_size(j) * (SC // 2 * k + t // 2 + 1))
                n = NTR * t + j
                if not (first and n < 2):
                    pe.wait_ge(tr_sb[n % 2], (NTR * SC // 2) * k + fills(n % 2, n))
                for i in range(fill_size(j)):
                    done = pe.transpose(ps_tr[:, n % 2, i * TILE:(i + 1) * TILE], rows[:, t % 2, TRF * j + i, :], ident[:])
                done.then_inc(tr_ps, 1)

            def interactions(k, first, t, q):
                tile = SC * k + t
                if q == 0:
                    done = NTR * (t + 1)
                    pe.wait_ge(tr_sb[0], (NTR * SC // 2) * k + fills(0, done))
                    pe.wait_ge(tr_sb[1], (NTR * SC // 2) * k + fills(1, done))
                    pe.wait_ge(side, 2 * (tile + 1))
                if not (first and t == 0 and q < 2):
                    pe.wait_ge(gr_sb[q % 2], NGR // 2 * tile + q // 2)
                for i in range(GPB):
                    four = feat[:, t % 2, q * GPB + i].rearrange("d s f -> d (s f)")
                    last = pe.matmul(ps_gr[0:S4 * F, q % 2, i * S4 * F:(i + 1) * S4 * F], four, four,
                                     start=True, stop=True)
                last.then_inc(gr_ps, 1)

            def layer1(tile, par, n_par, pool_share=False):
                for a in range(-1, NP3):
                    if pool_share and a == NP3 - 1:
                        pe.wait_ge(pairs_in_pool, 16 * S4)
                    elif a >= 0:
                        pe.wait_ge(pairs_in[par][a], PRW * n_par)
                    for c in range(HID1 // 128):
                        cols = slice(c * 128, (c + 1) * 128)
                        if a < 0:
                            pe.matmul(ps_l1[:, cols], wds[:, cols], dense[:, bass.ds(tile * TILE, TILE)],
                                      start=(c == 0), stop=False)
                        else:
                            done = pe.matmul(ps_l1[:, cols], wp[:, a, cols], pairs[:, par, a, :],
                                             start=False, stop=(a == NP3 - 1 and c == HID1 // 128 - 1))
                done.then_inc(l1_ps, 1)

            def layer2(tile):
                for m in range(HID2 // 128):
                    for c in range(HID1 // 128):
                        if m == 0:
                            pe.wait_ge(l1_sb, HID1 // 128 * tile + c + 1)
                        done = pe.matmul(ps_l2[:, m * TILE:(m + 1) * TILE], w2s[:, c, m * 128:(m + 1) * 128], h1[:, c, :],
                                         start=(c == 0), stop=(c == HID1 // 128 - 1))
                done.then_inc(l2_ps, 1)

            def layer3(tile):
                pe.wait_ge(l2_sb, HID2 // 128 * (tile + 1))
                for m in range(HID2 // 128):
                    last = pe.matmul(ps_l2[0:1, HID2:HID2 + TILE], w3s[:, m:m + 1], h2[:, m, :],
                                     start=(m == 0), stop=(m == HID2 // 128 - 1))
                last.then_inc(l3_ps, 1)

            def rest_of_mlp(tile, with_layer1):
                if with_layer1:
                    pe.wait_ge(l1_sb, HID1 // 128 * tile)
                    layer1(tile, tile % 2, tile // 2 + 1, tile == TILES - 1)
                pe.wait_ge(y_sb, tile)
                layer2(tile)
                layer3(tile)

            def superchunk(k, first, last):
                for t in range(SC):
                    tile = SC * k + t
                    mlp = not (first and t < 2) and not (last and t == SC - 1)
                    for q in range(NGR):
                        interactions(k, first, t, q)
                        if mlp and q == Q_L1:
                            if first and t == 2:
                                pe.wait_ge(w_in, W_IN)
                                pe.wait_ge(wds_ok, 1)
                            else:
                                pe.wait_ge(l1_sb, HID1 // 128 * (tile - 2))
                            layer1(tile - 2, t % 2, 2 * k + t // 2)
                        if 0 <= q - Q_TR < NTR and not (last and t >= SC - 2):
                            transposes(k, first, t + 1, q - Q_TR)
                        m = NGR * t + q - U_PICK
                        if not last and 0 <= m < NB:
                            pick(k + 1, m // BATCHES, m % BATCHES, True)
                        if mlp and q == Q_L2:
                            if not (first and t == 2):
                                pe.wait_ge(y_sb, tile - 2)
                            layer2(tile - 2)
                        if mlp and q == Q_L3:
                            layer3(tile - 2)
                    if last and t == SC - 2:
                        pe.wait_ge(l1_sb, HID1 // 128 * (tile - 1))
                        layer1(tile - 1, (t + 1) % 2, 2 * k + (t + 1) // 2)
                        for j in range(NTR):
                            transposes(k, first, t + 1, j)

            pe.wait_ge(ident1, 1)
            for n in range(NO):
                for h in range(BATCHES):
                    pick(0, n, h, False)
                for j in range(NTR):
                    if TR0_BEHIND[j] == n:
                        transposes(0, True, 0, j)
            superchunk(0, True, False)
            with pe.Fori(1, SUPERS - 1) as k:
                superchunk(k, False, False)
            superchunk(SUPERS - 1, False, True)
            for tile in range(TILES - 3, TILES):
                rest_of_mlp(tile, tile > TILES - 3)


def kernel(**inputs):
    import concourse.bacc as bacc
    from concourse.bass_utils import run_bass_kernel_spmd

    a = {n: np.asarray(v) for n, v in inputs.items()}
    pair_row = np.zeros((F, F), np.int64)
    i0, i1 = np.triu_indices(F, k=1)
    pair_row[i0, i1] = D + np.arange(len(i0))
    order = []
    for i in range(F):
        for k in range(1, HALF + 1):
            i_ref, j_ref = ORDER[i], ORDER[(i + k) % F]
            order.append(pair_row[min(i_ref, j_ref), max(i_ref, j_ref)])
    w1 = a["W_top1"]
    n_pairs = len(order)
    arrays = {
        "dense_t": a["r_dense_features"].T,
        "idx_rows": a["ids"][:, GATHERED].reshape(TILES, TILE, NG).transpose(1, 0, 2).reshape(TILE, TILES * NG),
        "ids_onehot": a["ids"][:, ONEHOT].T,
        "w_dense": np.concatenate([w1[:D], w1[D + n_pairs:]]),
        "w_pairs": w1[np.array(order)],
        "b1": a["b_top1"], "w2": a["W_top2"], "b2": a["b_top2"], "w3": a["W_top3"],
    }
    arrays.update({f"tbl_{f}": a[f"tbl_{f}"] for f in range(N_TABLES)})
    arrays = {n: np.ascontiguousarray(v) for n, v in arrays.items()}

    nc = bacc.Bacc("TRN2", target_bir_lowering=False, num_devices=1)
    ap = {n: nc.dram_tensor(n, v.shape, mybir.dt.from_np(v.dtype), kind="ExternalInput").ap() for n, v in arrays.items()}
    out = nc.dram_tensor("y_out", (BATCH, 1), FP32, kind="ExternalOutput").ap()
    dlrm_tower(nc, ap["dense_t"], ap["idx_rows"], ap["ids_onehot"], [ap[f"tbl_{f}"] for f in range(N_TABLES)],
               ap["w_dense"], ap["w_pairs"], ap["b1"], ap["w2"], ap["b2"], ap["w3"], out)
    r = run_bass_kernel_spmd(nc, [arrays], core_ids=[0])
    return r.results[0]["y_out"]
```
